# Optimizing a Trainium2 kernel written in Bass

```python
import numpy as np
import jax
import jax.numpy as jnp

def _softmax(x, axis=-1):
    return jax.nn.softmax(x, axis=axis)

def _gelu(x):
    return jax.nn.gelu(x, approximate=True)

def _silu(x):
    return jax.nn.silu(x)

def _sigmoid(x):
    return jax.nn.sigmoid(x)

def _layernorm(x, axis=-1, eps=1e-05):
    m = jnp.mean(x, axis=axis, keepdims=True)
    v = jnp.var(x, axis=axis, keepdims=True)
    return (x - m) / jnp.sqrt(v + eps)

def _scatter_add(tgt, idx, src, axis=0):
    return tgt.at[idx].add(src)

def _segment_sum(src, seg, n):
    return jax.ops.segment_sum(src, seg, n)
kernel_name = 'mk_adj_resnorm_d1_adj_r2_a34b3f'

def setup_inputs(seed: int=0):
    np.random.seed(seed)
    _w = jnp.asarray

    def _rec_inputs():
        import jax
        import jax.numpy as jnp
        _gk = jax.random.key(seed)
        x = -0.000929 + 1 * jax.random.normal(jax.random.fold_in(_gk, 1), (8, 1024, 128), jnp.float32)
        _a = jax.random.bernoulli(jax.random.fold_in(_gk, 2), 0.015625, (8, 1024, 1024))
        adj = _a.astype(jnp.int32)
        return (x, adj)
    x, adj = _rec_inputs()

    def _L0_gnn_setup():
        import jax, jax.numpy as jnp
        import numpy as np
        B, N, E, H = (2, 1024, 128, 4)
        DK = E // H
        key = jax.random.key(seed)
        ks = jax.random.split(key, 7)
        xav = lambda k, shape, fan_in, fan_out: jax.random.uniform(k, shape, minval=-1.0, maxval=1.0, dtype=jnp.float32) * np.sqrt(6.0 / (fan_in + fan_out))
        return {'node_embeddings': jax.random.normal(ks[0], (B, N, E), dtype=jnp.float32), 'adjacency_matrices': jax.random.randint(ks[1], (B, N, N), 0, 2, dtype=jnp.int32), 'Wq': xav(ks[2], (H, E, DK), E, DK), 'Wk': xav(ks[3], (H, E, DK), E, DK), 'Wv': xav(ks[4], (H, E, DK), E, DK), 'Wo': xav(ks[5], (E, E), E, E), 'bo': jnp.zeros((E,), dtype=jnp.float32)}
    _L0_gnn_all = _L0_gnn_setup()
    _L0_gnn_in = {k: v for k, v in _L0_gnn_all.items() if k in ('Wq', 'Wk', 'Wv', 'Wo', 'bo')}
    del _L0_gnn_all
    return {'x': x, 'adj': adj, 'L0_gnn_Wq': _L0_gnn_in['Wq'], 'L0_gnn_Wk': _L0_gnn_in['Wk'], 'L0_gnn_Wv': _L0_gnn_in['Wv'], 'L0_gnn_Wo': _L0_gnn_in['Wo'], 'L0_gnn_bo': _L0_gnn_in['bo']}

def reference(x, adj, L0_gnn_Wq, L0_gnn_Wk, L0_gnn_Wv, L0_gnn_Wo, L0_gnn_bo):
    import jax
    import jax.numpy as jnp

    def _L0_gnn_ref(node_embeddings, adjacency_matrices, Wq, Wk, Wv, Wo, bo):
        import jax, jax.numpy as jnp
        import numpy as np
        B, N, E, H = (2, 1024, 128, 4)
        DK = E // H
        Q = jnp.einsum('bnd,hde->bhne', node_embeddings, Wq)
        K = jnp.einsum('bnd,hde->bhne', node_embeddings, Wk)
        V = jnp.einsum('bnd,hde->bhne', node_embeddings, Wv)
        scale = 1.0 / np.sqrt(DK).astype(np.float32)
        scores = jnp.einsum('bhne,bhme->bhnm', Q, K) * scale
        mask = adjacency_matrices[:, None, :, :] > 0
        scores = jnp.where(mask, scores, -jnp.inf)
        attn = jax.nn.softmax(scores, axis=-1)
        heads = jnp.einsum('bhnm,bhme->bhne', attn, V)
        concat = heads.transpose(0, 2, 1, 3).reshape(node_embeddings.shape[0], node_embeddings.shape[1], E)
        return concat @ Wo.T + bo
    x = _layernorm(x + _L0_gnn_ref(x, adj, L0_gnn_Wq, L0_gnn_Wk, L0_gnn_Wv, L0_gnn_Wo, L0_gnn_bo), axis=-1)
    return x

_drawn_inputs = setup_inputs


def setup_inputs(seed=0):
    import zlib

    import numpy as np

    out = dict(_drawn_inputs(seed))
    spreads = {'L0_gnn_bo': (0.0, 0.1)}
    factors = {}
    for name, (base, spread) in spreads.items():
        noise = np.random.default_rng([zlib.crc32(name.encode()), seed]).standard_normal(out[name].shape)
        drawn = base * np.exp(spread * noise) if base else spread * noise
        out[name] = jnp.asarray(drawn.astype(out[name].dtype))
    for name, factor in factors.items():
        out[name] = (out[name] * factor).astype(out[name].dtype)
    return out
```

```python
from contextlib import ExitStack

import concourse.bass as bass
from concourse import mybir

F32 = mybir.dt.float32
F32R = mybir.dt.float32r
BF16 = mybir.dt.bfloat16
I32 = mybir.dt.int32
ALU = mybir.AluOpType
ACT = mybir.ActivationFunctionType

P = 128
MASKED = -1e30
LOWEST = -1e20
EPS = 1e-5


def build_kernel(nc, x, adj, wq, wk, wv, wo_t, bo, out):
    B, N, E = x.shape
    H = wq.shape[1] // 32
    DK = E // H
    SCALE = float(DK) ** -0.5
    HALF = 512
    STEPS = B * N // HALF
    NB = HALF // P
    MT = N // P
    TILES = MT * H
    RING = 2
    SHIFT_ROW = 3 * DK
    STACK_DMAS = 3 * H * 2
    assert (E, H, DK, N) == (128, 4, 32, 1024)

    x_blocks = x.rearrange("b (t p) e -> (b t) p e", p=P)
    adj_blocks = adj.rearrange("b (t p) m -> (b t) p m", p=P)
    x_steps = x.rearrange("b (t c p) e -> (b t) p c e", p=P, c=NB)
    out_steps = out.rearrange("b (t c p) e -> (b t) p c e", p=P, c=NB)
    x_graphs = x.rearrange("b (t p) e -> b p t e", p=P)

    def order(s):
        after = {j: [] for j in range(TILES)}
        if s < STEPS - 1:
            for i in range(NB * H):
                after[i * 26 // (NB * H)].append(("max", i // H, i % H))
            after[28].append(("shift",))
        if s % 2 == 0 and s < STEPS - 2:
            after[5].append(("x_t",))
            after[9].append(("q",))
            after[12].append(("k",))
            after[15].append(("v",))
        if s >= 1:
            after[3].append(("drain",))
            for c in range(NB):
                after[5 + 2 * c].append(("recip", c))
            after[21].append(("project",))
            after[26].append(("norm",))
        items = []
        for j in range(TILES):
            items.append(("scores", j))
            if j % H == H - 1:
                g = j // H - 1
                if g >= 0:
                    items.append(("values", s, g))
                elif s >= 1:
                    items.append(("values", s - 1, MT - 1))
            items += after[j]
        return items

    JOBS = ("max", "shift", "x_t", "q", "k", "v", "project")
    BEFORE = [("x_t",), ("q",), ("k",), ("v",)] + [("max", c, h) for c in range(NB) for h in range(H)] + [("shift",)]
    AFTER = [("values", STEPS - 1, MT - 1), ("drain",)] + [("recip", c) for c in range(NB)] + [("project",), ("norm",)]

    def jobs_in(items):
        return sum(i[0] in JOBS for i in items)

    first_job = {-1: 0, 0: jobs_in(BEFORE)}
    for s in range(STEPS):
        first_job[s + 1] = first_job[s] + jobs_in(order(s))
    LOOP = 3
    PER = first_job[6] - first_job[2]
    assert PER == first_job[10] - first_job[6] == first_job[14] - first_job[10] and PER % 2 == 0

    shift_dram = nc.dram_tensor("shift_dram", (H * NB, P), F32, kind="Internal").ap()

    with ExitStack() as ctx:
        def sb(name, shape, dt):
            return ctx.enter_context(nc.sbuf_tensor(name, shape, dt))

        def sem(name):
            return ctx.enter_context(nc.semaphore(name))

        ident = sb("ident", [P, P], F32)
        ident_bf = sb("ident_bf", [P, P], BF16)
        ones = sb("ones", [P, DK], F32)
        wq_sb = sb("wq_sb", [P, P], F32)
        wk_sb = sb("wk_sb", [P, P], F32)
        wv_sb = sb("wv_sb", [P, P], F32)
        wo_sb = sb("wo_sb", [P, P], F32)
        bo_sb = sb("bo_sb", [P, NB, E], F32)
        minus_half = sb("minus_half", [P, NB], F32)
        adj_in = sb("adj_in", [P, NB, N], I32)
        mask = sb("mask", [P, 4, NB, N], BF16)
        x_in = sb("x_in", [P, MT, E], F32)
        x_t = sb("x_t", [P, N], F32)
        q_hi = sb("q_hi", [P, N], F32R)
        q_lo = sb("q_lo", [P, N], F32R)
        k_hi = sb("k_hi", [P, N], F32R)
        k_lo = sb("k_lo", [P, N], F32R)
        q_stack = [sb(f"q_stack{i}", [SHIFT_ROW + 1, 2, H, HALF], F32R) for i in range(2)]
        k_stack = [sb(f"k_stack{i}", [SHIFT_ROW + 1, H, N], F32R) for i in range(2)]
        values = [sb(f"values{i}", [P, MT, P], F32) for i in range(2)]
        masked_scores = sb("masked_scores", [P, 2, N], BF16)
        row_max = sb("row_max", [P, H, NB], F32)
        shift_t = sb("shift_t", [H * NB, P], F32R)
        probs = sb("probs", [P, RING, H, HALF], F32)
        heads_sum = sb("heads_sum", [P, HALF], F32)
        denoms = sb("denoms", [P, HALF], F32)
        recips = sb("recips", [P, HALF], F32)
        concat = sb("concat", [P, HALF], F32)
        x_res = sb("x_res", [P, NB, E], F32)
        res_bias = sb("res_bias", [P, NB, E], F32)
        y = sb("y", [P, NB, E], F32)
        stats = sb("stats", [P, NB, 6], F32)
        moments = sb("moments", [P, NB, 2], F32)
        var_eps = sb("var_eps", [P, NB], F32)
        rstd = sb("rstd", [P, NB], F32)
        y_norm = sb("y_norm", [P, 2, NB, E], F32)

        job = [ctx.enter_context(nc.psum_tensor(f"job{i}", [P, N], F32)) for i in range(2)]
        scores = [ctx.enter_context(nc.psum_tensor(f"scores{i}", [P, HALF], F32)) for i in range(2)]
        heads_acc = ctx.enter_context(nc.psum_tensor("heads_acc", [P, HALF], F32))
        denom_acc = ctx.enter_context(nc.psum_tensor("denom_acc", [P, HALF], F32))

        weights_loaded = sem("weights_loaded")
        x_loaded = sem("x_loaded")
        res_loaded = sem("res_loaded")
        adj_loaded = [sem(f"adj_loaded{i}") for i in range(NB)]
        stacks_loaded = sem("stacks_loaded")
        shift_out = sem("shift_out")
        shift_loaded = sem("shift_loaded")
        stored = [sem(f"stored{i}") for i in range(2)]
        fills = sem("fills")
        consts = sem("consts")
        masks_made = sem("masks_made")
        job_full = [sem(f"job_full{i}") for i in range(2)]
        job_free = [sem(f"job_free{i}") for i in range(2)]
        scores_ready = sem("scores_ready")
        probs_ready = sem("probs_ready")
        values_done = sem("values_done")
        x_t_ready = sem("x_t_ready")
        hi_ready = sem("hi_ready")
        v_ready = sem("v_ready")
        lo_ready = sem("lo_ready")
        shift_t_ready = sem("shift_t_ready")
        drained = sem("drained")
        recips_ready = sem("recips_ready")
        res_bias_ready = sem("res_bias_ready")
        concat_ready = sem("concat_ready")
        stats_ready = sem("stats_ready")
        moments_ready = sem("moments_ready")
        var_ready = sem("var_ready")
        rstd_ready = sem("rstd_ready")
        norm_ready = sem("norm_ready")

        waited = sem("waited")

        block = ctx.enter_context(nc.Block())

        def count(turn, s, per, more=0):
            n = max(per * s + more, 0)
            return n if isinstance(turn, int) else turn * (4 * per) + n

        def graphs(turn, s, per, more=0):
            n = max(per * (s // 2) + more, 0)
            return n if isinstance(turn, int) else turn * (2 * per) + n

        def settle(eng, turn):
            if not isinstance(turn, int):
                eng.sem_inc(waited, 1)

        def uses(turn, n):
            return n // 2 if isinstance(turn, int) else turn * (PER // 2) + n // 2

        def run(eng, part):
            def items(turn, s, listed):
                n = first_job[s]
                for item in listed:
                    part(turn, s, item, n)
                    n += item[0] in JOBS

            items(0, -1, BEFORE)
            for s in range(2):
                items(0, s, order(s))
            with eng.Fori(0, LOOP) as turn:
                for s in range(2, 6):
                    items(turn, s, order(s))
            for s in range(4 * LOOP + 2, STEPS):
                items(0, s, order(s))
            items(0, STEPS, AFTER)

        @block.sync
        def _(sp):
            def load_adj(step, c, before, masks):
                sp.wait_ge(masks_made, masks)
                sp.dma_start(adj_in[:, c, :], before).then_inc(adj_loaded[c], 16)

            sp.dma_start(x_in[:], x_graphs[0]).then_inc(x_loaded, 16)
            sp.dma_start(wq_sb[:], wq).then_inc(weights_loaded, 16)
            sp.dma_start(wk_sb[:], wk).then_inc(weights_loaded, 16)
            for c in range(NB):
                sp.dma_start(adj_in[:, c, :], adj_blocks[c]).then_inc(adj_loaded[c], 16)
            sp.dma_start(wv_sb[:], wv).then_inc(weights_loaded, 16)
            sp.dma_start(wo_sb[:], wo_t).then_inc(weights_loaded, 16)
            for c in range(NB):
                sp.dma_start(bo_sb[:, c, :], bo.partition_broadcast(P)).then_inc(weights_loaded, 16)

            def stacks(turn, s, which):
                hi, lo = (q_hi, q_lo) if which == "q" else (k_hi, k_lo)
                par = ((s + 2) // 2) % 2
                sp.wait_ge(lo_ready, graphs(turn, s + 2, 2, 1 if which == "q" else 2))
                settle(sp, turn)
                if s >= 1:
                    sp.wait_ge(scores_ready, count(turn, s, TILES))
                    settle(sp, turn)
                for row, part in enumerate((hi, lo, hi) if which == "q" else (hi, hi, lo)):
                    for h in range(H):
                        src = part[DK * h:DK * h + DK, :].bitcast(F32)
                        if which == "q":
                            dst = q_stack[par][DK * row:DK * row + DK, :, h, :].bitcast(F32)
                            src = src.rearrange("p (t n) -> p t n", t=2)
                        else:
                            dst = k_stack[par][DK * row:DK * row + DK, h, :].bitcast(F32)
                        sp.dma_start(dst, src).then_inc(stacks_loaded, 16)

            def part(turn, s, item, n):
                if item == ("scores", 0) and s % 2 == 0 and s < STEPS - 2:
                    sp.wait_ge(x_t_ready, graphs(turn, s + 2, 1))
                    settle(sp, turn)
                    sp.dma_start(x_in[:], x_graphs[graphs(turn, s + 2, 1)]).then_inc(x_loaded, 16)
                if item[0] in "qk":
                    stacks(turn, s if s >= 0 else -2, item[0])
                if item[0] == "v" and s == -1:
                    more_adj(turn, -1)
                if item == ("scores", 0) and s < STEPS - 2:
                    more_adj(turn, s)
                if item[0] == "shift":
                    sp.wait_ge(shift_t_ready, count(turn, s + 1, 1, 1))
                    settle(sp, turn)
                    sp.dma_start(shift_dram, shift_t[:].bitcast(F32)).then_inc(shift_out, 16)
                    sp.wait_ge(shift_out, count(turn, s + 1, 16, 16))
                    settle(sp, turn)
                    dst = q_stack[((s + 1) // 2) % 2][SHIFT_ROW:SHIFT_ROW + 1, (s + 1) % 2, :, :]
                    sp.dma_start(dst.bitcast(F32).rearrange("p h n -> p (h n)"),
                                 shift_dram.rearrange("(o r) n -> o (r n)", o=1)).then_inc(shift_loaded, 16)
                if item == ("scores", 2):
                    sp.wait_ge(res_bias_ready, count(turn, s, 1))
                    settle(sp, turn)
                    sp.dma_start(x_res[:], x_steps[count(turn, s, 1)]).then_inc(res_loaded, 16)
                if item[0] == "norm":
                    sp.wait_ge(norm_ready, count(turn, s, NB))
                    k = (s - 1) % 2
                    settle(sp, turn)
                    sp.dma_start(out_steps[count(turn, s, 1, -1)], y_norm[:, k]).then_inc(stored[k], 16)

            def more_adj(turn, s):
                for c in range(NB):
                    sp.wait_ge(masks_made, count(turn, s, NB, NB + c + 1))
                    settle(sp, turn)
                    sp.dma_start(adj_in[:, c, :], adj_blocks[count(turn, s, NB, 2 * NB + c)]).then_inc(adj_loaded[c], 16)

            run(sp, part)
            for k in range(2):
                sp.wait_ge(stored[k], 16 * STEPS // 2)

        @block.gpsimd
        def _(pool):
            for k, t in enumerate((ident, ident_bf)):
                nc.gpsimd.memset(t[:], 0.0).then_inc(consts, 1)
                pool.wait_ge(consts, 2 * k + 1)
                nc.gpsimd.affine_select(out=t[:], in_=t[:], compare_op=ALU.not_equal, fill=1.0, base=0,
                                        pattern=[[-1, P]], channel_multiplier=1).then_inc(consts, 1)

            def make_mask(turn, s, c):
                pool.wait_ge(adj_loaded[c], count(turn, s, 16, 16))
                if s >= 4:
                    pool.wait_ge(scores_ready, count(turn, s - 3, TILES))
                settle(pool, turn)
                nc.gpsimd.tensor_scalar(mask[:, s % 4, c, :], adj_in[:, c, :], 0, MASKED,
                                        ALU.is_le, ALU.mult).then_inc(masks_made, 1)

            def part(turn, s, item, n):
                if s == -1:
                    if item[0] == "x_t":
                        for c in range(NB):
                            make_mask(turn, 0, c)
                    return
                if s == 0 and item == ("scores", 0):
                    for c in range(NB):
                        make_mask(turn, 1, c)
                if item[0] == "scores" and item[1] in (2, 11, 17, 23) and s < STEPS - 2:
                    make_mask(turn, s + 2, (2, 11, 17, 23).index(item[1]))
                if item[0] == "drain":
                    pool.wait_ge(res_loaded, count(turn, s, 16))
                    pool.wait_ge(weights_loaded, 16 * 8)
                    pool.wait_ge(moments_ready, count(turn, s - 1, NB))
                    nc.gpsimd.tensor_tensor(res_bias[:], x_res[:], bo_sb[:], ALU.add).then_inc(res_bias_ready, 1)
                if item == ("recip", NB - 1):
                    pool.wait_ge(recips_ready, count(turn, s, NB))
                    pool.wait_ge(drained, count(turn, s, 2))
                    nc.gpsimd.tensor_tensor(concat[:], heads_sum[:], recips[:], ALU.mult).then_inc(concat_ready, 1)
                if item[0] == "norm":
                    pool.wait_ge(moments_ready, count(turn, s, NB))
                    if s > 1:
                        pool.wait_ge(norm_ready, count(turn, s - 1, NB))
                    settle(pool, turn)
                    nc.gpsimd.tensor_scalar(var_eps[:], moments[:, :, 1], EPS, None, ALU.add).then_inc(var_ready, 1)
                    pool.wait_ge(var_ready, count(turn, s, 1))
                    pool.wait_ge(fills, 4)
                    nc.gpsimd.tensor_tensor(rstd[:], var_eps[:], minus_half[:], ALU.pow).then_inc(rstd_ready, 1)

            run(pool, part)

        @block.tensor
        def _(pe):
            pe.wait_ge(fills, 4)
            pe.wait_ge(consts, 4)
            pe.wait_ge(weights_loaded, 16 * 8)

            def part(turn, s, item, n):
                kind = item[0]
                if kind == "scores":
                    mt, h = item[1] // H, item[1] % H
                    par, half = (s // 2) % 2, s % 2
                    t = item[1]
                    if t == 0:
                        pe.wait_ge(shift_loaded, count(turn, s, 16, 16))
                    pe.wait_ge(probs_ready, count(turn, s, TILES, t - 1))
                    bank = scores[t % 2]
                    nc.tensor.matmul(bank[:], k_stack[par][:, h, mt * P:mt * P + P], q_stack[par][:, half, h, :],
                                     start=True, stop=False, skip_group_check=True)
                    for c in range(NB):
                        last = nc.tensor.matmul(bank[:, c * P:c * P + P], mask[:, s % 4, c, mt * P:mt * P + P],
                                                ident_bf[:], start=False, stop=(c == NB - 1), skip_group_check=True)
                    last.then_inc(scores_ready, 1)
                if kind == "values":
                    at, g = item[1], item[2]
                    d = at - s
                    pe.wait_ge(probs_ready, count(turn, s, TILES, d * TILES + H * (g + 1)))
                    if g == 0:
                        pe.wait_ge(drained, count(turn, s, 2))
                        pe.wait_ge(v_ready, graphs(turn, s - s % 2, 1, 1))
                    for h in range(H):
                        nc.tensor.matmul(heads_acc[DK * h:DK * h + DK, :],
                                         values[(at // 2) % 2][:, g, DK * h:DK * h + DK], probs[:, g % RING, h, :],
                                         start=(g == 0), stop=(g == MT - 1))
                    for h in range(H):
                        last = nc.tensor.matmul(denom_acc[DK * h:DK * h + DK, :], ones[:], probs[:, g % RING, h, :],
                                                start=(g == 0), stop=(g == MT - 1))
                    last.then_inc(values_done, 1)
                if kind not in JOBS:
                    return
                slot = n % 2
                pe.wait_ge(job_free[slot], uses(turn, n))
                if kind == "max":
                    c, h = item[1:]
                    nxt = s + 1
                    if (c, h) == (0, 0) and nxt % 2 == 0:
                        pe.wait_ge(stacks_loaded, graphs(turn, nxt, 16 * STACK_DMAS, 16 * STACK_DMAS))
                    q_t, k_t = q_stack[(nxt // 2) % 2], k_stack[(nxt // 2) % 2]
                    for i in range(2):
                        last = nc.tensor.matmul(job[slot][:, i * HALF:i * HALF + HALF],
                                                q_t[0:SHIFT_ROW, nxt % 2, h, c * P:c * P + P],
                                                k_t[0:SHIFT_ROW, h, i * HALF:i * HALF + HALF], start=True, stop=True)
                elif kind == "shift":
                    pe.wait_ge(job_free[1 - slot], uses(turn, n + 1))
                    last = nc.tensor.transpose(job[slot][0:H * NB, 0:P], row_max[:], ident[:])
                elif kind == "x_t":
                    pe.wait_ge(x_loaded, graphs(turn, s + 2 if s >= 0 else 0, 16, 16))
                    for t in range(MT):
                        last = nc.tensor.transpose(job[slot][:, t * P:t * P + P], x_in[:, t, :], ident[:])
                elif kind in "qk":
                    if kind == "q":
                        pe.wait_ge(x_t_ready, graphs(turn, s + 2 if s >= 0 else 0, 1, 1))
                    for i in range(2):
                        last = nc.tensor.matmul(job[slot][:, i * HALF:i * HALF + HALF], (wq_sb if kind == "q" else wk_sb)[:],
                                                x_t[:, i * HALF:i * HALF + HALF], start=True, stop=True)
                elif kind == "v":
                    for t in range(MT):
                        last = nc.tensor.matmul(job[slot][:, t * P:t * P + P], x_t[:, t * P:t * P + P], wv_sb[:],
                                                start=True, stop=True)
                elif kind == "project":
                    pe.wait_ge(concat_ready, count(turn, s, 1))
                    for c in range(NB):
                        last = nc.tensor.matmul(job[slot][:, c * E:c * E + E], concat[:, c * P:c * P + P], wo_sb[:],
                                                start=True, stop=True)
                last.then_inc(job_full[slot], 1)

            run(pe, part)

        @block.scalar
        def _(act):
            def part(turn, s, item, n):
                kind, slot = item[0], n % 2
                if kind == "scores":
                    t = item[1]
                    act.wait_ge(scores_ready, count(turn, s, TILES, t + 1))
                    if t % H == 0:
                        act.wait_ge(values_done, count(turn, s, MT, t // H - RING + 1))
                    nc.scalar.activation(probs[:, (t // H) % RING, t % H, :], scores[t % 2][:], ACT.Exp,
                                         scale=SCALE).then_inc(probs_ready, 1)
                if kind == "drain":
                    act.wait_ge(values_done, count(turn, s, MT))
                    act.wait_ge(concat_ready, count(turn, s, 1, -1))
                    nc.scalar.copy(heads_sum[:], heads_acc[:]).then_inc(drained, 1)
                    nc.scalar.copy(denoms[:], denom_acc[:]).then_inc(drained, 1)
                if kind in ("shift", "x_t", "q", "k", "v"):
                    act.wait_ge(job_full[slot], uses(turn, n + 2))
                if kind == "shift":
                    act.wait_ge(shift_loaded, count(turn, s + 1, 16))
                    nc.scalar.mul(shift_t[:], job[slot][0:H * NB, 0:P], -1.0).then_inc(shift_t_ready, 1)
                if kind == "x_t":
                    nc.scalar.copy(x_t[:], job[slot][:]).then_inc(x_t_ready, 1)
                if kind in "qk":
                    act.wait_ge(stacks_loaded, graphs(turn, s + 2 if s >= 0 else 0, 16 * STACK_DMAS))
                    nc.scalar.copy((q_hi if kind == "q" else k_hi)[:], job[slot][:]).then_inc(hi_ready, 1)
                if kind == "v":
                    if s >= 2:
                        act.wait_ge(values_done, count(turn, s, MT))
                    g = (s + 2) // 2 if s >= 0 else 0
                    nc.scalar.copy(values[g % 2][:].rearrange("p t e -> p (t e)"), job[slot][:]).then_inc(v_ready, 1)
                if kind in ("shift", "x_t", "v"):
                    ready, per = {"shift": (shift_t_ready, count(turn, s + 1, 1, 1)),
                                  "x_t": (x_t_ready, graphs(turn, s + 2 if s >= 0 else 0, 1, 1)),
                                  "v": (v_ready, graphs(turn, s + 2 if s >= 0 else 0, 1, 1))}[kind]
                    act.wait_ge(ready, per)
                    act.sem_inc(job_free[slot], 1)

            run(act, part)

        @block.vector
        def _(dve):
            nc.vector.memset(ones[:], 1.0).then_inc(fills, 1)
            nc.vector.memset(minus_half[:], -0.5).then_inc(fills, 1)
            for i in range(2):
                nc.vector.memset(k_stack[i][SHIFT_ROW:SHIFT_ROW + 1].bitcast(F32), 1.0).then_inc(fills, 1)

            def part(turn, s, item, n):
                kind, slot = item[0], n % 2
                if kind in ("max", "project"):
                    dve.wait_ge(job_full[slot], uses(turn, n + 2))
                if kind == "max":
                    c, h = item[1:]
                    dve.wait_ge(masks_made, count(turn, s + 1, NB, c + 1))
                    settle(dve, turn)
                    nc.vector.tensor_tensor_reduce(out=masked_scores[:, slot, :], in0=job[slot][:],
                                                   in1=mask[:, (s + 1) % 4, c, :], scale=1.0, scalar=LOWEST,
                                                   op0=ALU.add, op1=ALU.max,
                                                   accum_out=row_max[:, h, c:c + 1]).then_inc(job_free[slot], 1)
                if kind in "qk":
                    g_hi = graphs(turn, s + 2 if s >= 0 else 0, 2, 1 if kind == "q" else 2)
                    dve.wait_ge(hi_ready, g_hi)
                    hi, lo = (q_hi, q_lo) if kind == "q" else (k_hi, k_lo)
                    nc.vector.tensor_tensor(lo[:], job[slot][:], hi[:].bitcast(F32), ALU.subtract).then_inc(lo_ready, 1)
                    dve.wait_ge(lo_ready, g_hi)
                    dve.sem_inc(job_free[slot], 1)
                if kind == "recip":
                    c = item[1]
                    dve.wait_ge(drained, count(turn, s, 2))
                    if c == 0:
                        dve.wait_ge(concat_ready, count(turn, s, 1, -1))
                    nc.vector.reciprocal(recips[:, c * P:c * P + P], denoms[:, c * P:c * P + P]).then_inc(recips_ready, 1)
                if kind == "project":
                    dve.wait_ge(res_bias_ready, count(turn, s, 1))
                    nc.vector.tensor_tensor(y[:], job[slot][:, 0:NB * E].rearrange("p (c e) -> p c e", c=NB),
                                            res_bias[:], ALU.add).then_inc(job_free[slot], 1)
                    dve.wait_ge(job_free[slot], uses(turn, n + 2))
                    for c in range(NB):
                        nc.vector.bn_stats(stats[:, c, :], y[:, c, :]).then_inc(stats_ready, 1)
                    for c in range(NB):
                        dve.wait_ge(stats_ready, count(turn, s - 1, NB, c + 1))
                        settle(dve, turn)
                        nc.vector.bn_aggr(moments[:, c, :], stats[:, c, :]).then_inc(moments_ready, 1)
                if kind == "norm":
                    dve.wait_ge(rstd_ready, count(turn, s, 1))
                    if s > 2:
                        dve.wait_ge(stored[(s - 1) % 2], stores(turn, s))
                    for c in range(NB):
                        nc.vector.tensor_scalar(y_norm[:, (s - 1) % 2, c, :], y[:, c, :], moments[:, c, 0:1],
                                                rstd[:, c:c + 1], ALU.subtract, ALU.mult).then_inc(norm_ready, 1)

            def stores(turn, s):
                n = 16 * ((s - 1) // 2)
                return n if isinstance(turn, int) else turn * 32 + n

            run(dve, part)


def kernel(x, adj, L0_gnn_Wq, L0_gnn_Wk, L0_gnn_Wv, L0_gnn_Wo, L0_gnn_bo):
    import numpy as np
    import concourse.bacc as bacc
    from concourse.bass_utils import run_bass_kernel_spmd

    def heads_last(w):
        return np.ascontiguousarray(np.transpose(np.asarray(w), (1, 0, 2)).reshape(w.shape[1], -1))

    arrays = {
        "x": np.ascontiguousarray(x),
        "adj": np.ascontiguousarray(adj),
        "wq": heads_last(L0_gnn_Wq),
        "wk": heads_last(L0_gnn_Wk),
        "wv": heads_last(L0_gnn_Wv),
        "wo_t": np.ascontiguousarray(np.asarray(L0_gnn_Wo).T),
        "bo": np.ascontiguousarray(L0_gnn_bo),
    }
    nc = bacc.Bacc("TRN2", target_bir_lowering=False, num_devices=1)
    args = [nc.dram_tensor(name, a.shape, mybir.dt.from_np(a.dtype), kind="ExternalInput").ap()
            for name, a in arrays.items()]
    out = nc.dram_tensor("out", x.shape, F32, kind="ExternalOutput").ap()
    build_kernel(nc, *args, out)
    r = run_bass_kernel_spmd(nc, [arrays], core_ids=[0])
    return r.results[0]["out"]
```

```python
from contextlib import ExitStack

import concourse.bass as bass
from concourse import mybir

F32 = mybir.dt.float32
F32R = mybir.dt.float32r
BF16 = mybir.dt.bfloat16
I32 = mybir.dt.int32
ALU = mybir.AluOpType
ACT = mybir.ActivationFunctionType

P = 128
MASKED = -1e28
LOWEST = -1e20
EPS = 1e-5


def build_kernel(nc, x, x_cols, adj, adj_cols, wq, wk, wv, wo_t, bo, out):
    B, N, E = x.shape
    H = wq.shape[1] // 32
    DK = E // H
    SCALE = float(DK) ** -0.5
    HALF = 512
    STEPS = B * N // HALF
    NB = HALF // P
    MT = N // P
    TILES = MT * H
    SUMMED = 4
    RING = 4
    SHIFT_ROW = 3 * DK
    STACK_DMAS = 3 * H * 2
    ADDS = (SUMMED - 1) * (MT // SUMMED)
    PAIRS = MT // 2
    assert (E, H, DK, N) == (128, 4, 32, 1024)

    adj_blocks = adj.rearrange("b (t p) m -> (b t) p m", p=P)
    adj_pairs = adj_cols.rearrange("b (i k p) (t q) -> b t i p k q", p=P, k=2, t=2)
    x_steps = x.rearrange("b (t c p) e -> (b t) p c e", p=P, c=NB)
    out_steps = out.rearrange("b (t c p) e -> (b t) p c e", p=P, c=NB)

    TABLE = [
        (1, ("max", 1, 1, 0)), (2, ("max", 1, 1, 1)), (2, ("mask_cols", 1, 0)), (3, ("max", 1, 1, 2)),
        (3, ("drain",)), (4, ("max", 1, 1, 3)), (6, ("q",)), (6, ("mask", 1, 2)), (6, ("mask", 1, 3)),
        (6, ("norm", 2)), (6, ("copy", "q")), (7, ("low", "q")), (7, ("mask_cols", 1, 1)),
        (8, ("max", 1, 2, 0)), (10, ("denoms",)), (10, ("k",)), (10, ("copy", "denoms")),
        (10, ("max", 1, 2, 1)), (10, ("copy", "k")), (12, ("low", "k")), (12, ("recip", 0)),
        (14, ("max", 1, 2, 2)), (14, ("max", 1, 2, 3)), (15, ("max", 1, 3, 0)), (15, ("recip", 1)),
        (17, ("max", 1, 3, 1)), (18, ("v",)), (18, ("copy", "v")), (19, ("max", 1, 3, 2)), (21, ("add", 1)),
        (21, ("max", 1, 3, 3)), (22, ("recip", 2)), (23, ("recip", 3)), (24, ("shift",)),
        (24, ("copy", "shift")), (24, ("add", 2)), (24, ("add", 3)), (25, ("mask", 2, 0)),
        (25, ("mask_cols", 1, 2)), (25, ("divide",)), (25, ("max", 2, 0, 0)), (25, ("add", 5)),
        (26, ("max", 2, 0, 1)), (27, ("project",)), (27, ("add", 6)), (27, ("mask", 2, 1)),
        (27, ("mask_cols", 1, 3)), (27, ("pow",)), (28, ("max", 2, 0, 2)), (29, ("max", 2, 0, 3)),
        (31, ("add", 7)),
    ]

    def order(s):
        after = {j: [] for j in range(TILES)}
        for j, item in TABLE:
            kind, arg = item[0], item[1] if len(item) > 1 else None
            if kind in ("q", "k", "v") or arg in ("q", "k", "v"):
                wanted = s % 2 == 0 and s < STEPS - 2
            elif kind in ("max", "mask"):
                wanted = s + arg < STEPS
            elif kind in ("mask_cols", "shift") or arg == "shift":
                wanted = s + 1 < STEPS
            elif kind == "norm":
                wanted = s >= 2
            else:
                wanted = s >= 1 or kind == "add"
            if wanted:
                after[j].append(item)
        items = []
        for j in range(TILES):
            items.append(("scores", j))
            if j % H == H - 1:
                g = j // H - 1
                if g >= 0:
                    items.append(("values", s, g))
                elif s >= 1:
                    items.append(("values", s - 1, MT - 1))
            items += after[j]
        return items

    JOBS = ("max", "shift", "q", "k", "v", "denoms", "project")
    BEFORE = ([("adj",), ("adj_cols",), ("q",), ("copy", "q"), ("k",), ("copy", "k"), ("low", "q"), ("low", "k"), ("v",), ("copy", "v")]
              + [("mask", 1, 0)]
              + [i for c in range(NB) for i in [("mask", 1 + (c + 1) // NB, (c + 1) % NB)] + [("max", 1, c, h) for h in range(H)]
                 + [("mask_cols", 1, c)]]
              + [("shift",), ("copy", "shift")] + [("max", 2, 0, h) for h in range(H)] + [("mask", 2, 1)])
    AFTER = ([("values", STEPS - 1, MT - 1), ("drain",), ("norm", 2), ("denoms",), ("copy", "denoms")]
             + [("recip", c) for c in range(NB)] + [("divide",), ("project",), ("pow",), ("norm", 1)])

    def jobs_in(items):
        return sum(i[0] in JOBS for i in items)

    first_job = {-1: 0, 0: jobs_in(BEFORE)}
    for s in range(STEPS):
        first_job[s + 1] = first_job[s] + jobs_in(order(s))
    LOOP = 3
    PER = first_job[6] - first_job[2]
    assert PER == first_job[10] - first_job[6] == first_job[14] - first_job[10] and PER % 2 == 0

    with ExitStack() as ctx:
        def sb(name, shape, dt):
            return ctx.enter_context(nc.sbuf_tensor(name, shape, dt))

        def sem(name):
            return ctx.enter_context(nc.semaphore(name))

        ident = sb("ident", [P, P], F32)
        minus_ident = sb("minus_ident", [P, P], BF16)
        ones = sb("ones", [P, DK], F32)
        wq_sb = sb("wq_sb", [P, P], F32)
        wk_sb = sb("wk_sb", [P, P], F32)
        wv_sb = sb("wv_sb", [P, P], F32)
        wo_sb = sb("wo_sb", [P, P], F32)
        bo_sb = sb("bo_sb", [P, E], F32)
        minus_half = sb("minus_half", [P, NB], F32)
        adj_in = sb("adj_in", [P, 2, N], I32)
        mask = sb("mask", [P, NB, N], BF16)
        adj_cols_in = sb("adj_cols_in", [P, 2, 2, HALF], I32)
        mask_cols = sb("mask_cols", [P, 2, MT, HALF], BF16)
        minus_masked = sb("minus_masked", [P, 1], F32)
        x_t = sb("x_t", [P, N], F32)
        q_hi = sb("q_hi", [P, N], F32R)
        q_lo = sb("q_lo", [P, N], F32R)
        k_hi = sb("k_hi", [P, N], F32R)
        k_lo = sb("k_lo", [P, N], F32R)
        q_stack = [sb(f"q_stack{i}", [SHIFT_ROW + 1, 2, H, HALF], F32R) for i in range(2)]
        k_stack = [sb(f"k_stack{i}", [SHIFT_ROW + 1, H, N], F32R) for i in range(2)]
        values = [sb(f"values{i}", [P, MT, P], F32) for i in range(2)]
        masked_scores = sb("masked_scores", [P, 2, N], BF16)
        row_max = sb("row_max", [P, H, NB], F32)
        shift_t = sb("shift_t", [NB, H * P], F32R)
        probs = sb("probs", [P, RING, H, HALF], F32)
        prob_sums = sb("prob_sums", [P, MT // SUMMED, H, HALF], F32)
        heads_sum = sb("heads_sum", [P, HALF], F32)
        denoms = sb("denoms", [P, HALF], F32)
        recips = sb("recips", [P, HALF], F32)
        concat = sb("concat", [P, HALF], F32)
        x_res = sb("x_res", [P, NB, E], F32)
        res_bias = sb("res_bias", [P, NB, E], F32)
        y = sb("y", [P, NB, E], F32)
        stats = sb("stats", [P, NB, 6], F32)
        moments = sb("moments", [P, NB, 2], F32)
        var_eps = sb("var_eps", [P, NB], F32)
        rstd = sb("rstd", [P, NB], F32)
        y_norm = sb("y_norm", [P, 2, NB, E], F32)

        job = [ctx.enter_context(nc.psum_tensor(f"job{i}", [P, N], F32)) for i in range(2)]
        scores = [ctx.enter_context(nc.psum_tensor(f"scores{i}", [P, HALF], F32)) for i in range(3)]
        heads_acc = ctx.enter_context(nc.psum_tensor("heads_acc", [P, HALF], F32))

        qk_weights_loaded = sem("qk_weights_loaded")
        weights_loaded = sem("weights_loaded")
        x_loaded = sem("x_loaded")
        res_loaded = sem("res_loaded")
        adj_loaded = [sem(f"adj_loaded{i}") for i in range(2)]
        adj_cols_loaded = [sem(f"adj_cols_loaded{i}") for i in range(2)]
        stacks_loaded = sem("stacks_loaded")
        shift_loaded = sem("shift_loaded")
        stored = [sem(f"stored{i}") for i in range(2)]
        sums_added = sem("sums_added")
        fills = sem("fills")
        consts = sem("consts")
        masks_made = sem("masks_made")
        mask_cols_made = sem("mask_cols_made")
        job_full = [sem(f"job_full{i}") for i in range(2)]
        job_free = [sem(f"job_free{i}") for i in range(2)]
        scores_ready = sem("scores_ready")
        probs_ready = sem("probs_ready")
        values_done = sem("values_done")
        hi_ready = sem("hi_ready")
        v_ready = sem("v_ready")
        lo_ready = sem("lo_ready")
        shift_t_ready = sem("shift_t_ready")
        drained = sem("drained")
        denoms_ready = sem("denoms_ready")
        recips_ready = sem("recips_ready")
        res_bias_ready = sem("res_bias_ready")
        concat_ready = sem("concat_ready")
        stats_ready = sem("stats_ready")
        moments_ready = sem("moments_ready")
        var_ready = sem("var_ready")
        rstd_ready = sem("rstd_ready")
        norm_ready = sem("norm_ready")

        waited = sem("waited")

        block = ctx.enter_context(nc.Block())

        def count(turn, s, per, more=0):
            n = max(per * s + more, 0)
            return n if isinstance(turn, int) else turn * (4 * per) + n

        def graphs(turn, s, per, more=0):
            n = max(per * (s // 2) + more, 0)
            return n if isinstance(turn, int) else turn * (2 * per) + n

        def settle(eng, turn):
            if not isinstance(turn, int):
                eng.sem_inc(waited, 1)

        def uses(turn, n):
            return n // 2 if isinstance(turn, int) else turn * (PER // 2) + n // 2

        def run(eng, part):
            def items(turn, s, listed):
                n, of = first_job[s], {}
                for item in listed:
                    if item[0] in JOBS:
                        of[item[0]] = n
                    part(turn, s, item, of[item[1]] if item[0] in ("copy", "low") else n)
                    n += item[0] in JOBS

            items(0, -1, BEFORE)
            for s in range(2):
                items(0, s, order(s))
            with eng.Fori(0, LOOP) as turn:
                for s in range(2, 6):
                    items(turn, s, order(s))
            for s in range(4 * LOOP + 2, STEPS):
                items(0, s, order(s))
            items(0, STEPS, AFTER)

        def fill_stack(eng, turn, s, which):
            to = s + 2 if s >= 0 else 0
            hi, lo = (q_hi, q_lo) if which == "q" else (k_hi, k_lo)
            eng.wait_ge(lo_ready, graphs(turn, to, 2, 1 if which == "q" else 2))
            settle(eng, turn)
            if s >= 1:
                eng.wait_ge(scores_ready, count(turn, s, TILES))
                settle(eng, turn)
            for h in range(H):
                for row, part in enumerate((hi, lo, hi) if which == "q" else (hi, hi, lo)):
                    src = part[DK * h:DK * h + DK, :].bitcast(F32)
                    if which == "q":
                        dst = q_stack[(to // 2) % 2][DK * row:DK * row + DK, :, h, :].bitcast(F32)
                        src = src.rearrange("p (t n) -> p t n", t=2)
                    else:
                        dst = k_stack[(to // 2) % 2][DK * row:DK * row + DK, h, :].bitcast(F32)
                    eng.dma_start(dst, src).then_inc(stacks_loaded, 16)

        @block.sync
        def _(sp):
            sp.dma_start(x_t[:], x_cols[0]).then_inc(x_loaded, 16)
            sp.dma_start(wq_sb[:], wq).then_inc(qk_weights_loaded, 16)
            sp.dma_start(wk_sb[:], wk).then_inc(qk_weights_loaded, 16)
            sp.dma_start(wv_sb[:], wv).then_inc(weights_loaded, 16)
            sp.dma_start(wo_sb[:], wo_t).then_inc(weights_loaded, 16)
            sp.dma_start(bo_sb[:], bo.partition_broadcast(P)).then_inc(weights_loaded, 16)

            def part(turn, s, item, n):
                if item == ("scores", 0) and s % 2 == 0 and s < STEPS - 2:
                    sp.wait_ge(v_ready, graphs(turn, s + 2, 1))
                    settle(sp, turn)
                    sp.dma_start(x_t[:], x_cols[graphs(turn, s + 2, 1)]).then_inc(x_loaded, 16)
                if item[0] == "low" and (item[1] == "q" or s >= 0):
                    fill_stack(sp, turn, s, item[1])
                if item[0] == "adj":
                    for c in range(2):
                        sp.dma_start(adj_in[:, c, :], adj_blocks[c]).then_inc(adj_loaded[c], 16)
                if item[0] == "mask":
                    to, c = s + item[1], item[2]
                    if to + (c + 2) // NB < STEPS:
                        sp.wait_ge(masks_made, count(turn, to, NB, c + 1))
                        settle(sp, turn)
                        sp.dma_start(adj_in[:, c % 2, :],
                                     adj_blocks[count(turn, to, NB, c + 2)]).then_inc(adj_loaded[c % 2], 16)
                if item[0] == "adj_cols":
                    for i in range(2):
                        sp.dma_start(adj_cols_in[:, i], adj_pairs[0, 0, i]).then_inc(adj_cols_loaded[i], 16)
                if item[0] == "mask_cols":
                    made, i = s + item[1], (item[2] + 2) % PAIRS
                    to = made + (item[2] + 2) // PAIRS
                    if to < STEPS:
                        sp.wait_ge(mask_cols_made, count(turn, made, PAIRS, item[2] + 1))
                        settle(sp, turn)
                        sp.dma_start(adj_cols_in[:, i % 2], adj_pairs[graphs(turn, to - to % 2, 1), to % 2, i]
                                     ).then_inc(adj_cols_loaded[i % 2], 16)
                if item == ("copy", "shift"):
                    sp.wait_ge(shift_t_ready, count(turn, s + 1, 1, 1))
                    settle(sp, turn)
                    for c in range(NB):
                        dst = q_stack[((s + 1) // 2) % 2][SHIFT_ROW:SHIFT_ROW + 1, (s + 1) % 2, :, c * P:c * P + P]
                        sp.dma_start(dst.bitcast(F32), shift_t[c:c + 1, :].bitcast(F32)
                                     .rearrange("p (h n) -> p h n", h=H)).then_inc(shift_loaded, 16)
                if item == ("scores", 2):
                    sp.wait_ge(res_bias_ready, count(turn, s, 1))
                    settle(sp, turn)
                    sp.dma_start(x_res[:], x_steps[count(turn, s, 1)]).then_inc(res_loaded, 16)
                if item[0] == "norm":
                    d = item[1]
                    sp.wait_ge(norm_ready, count(turn, s - d, NB, NB))
                    k = (s - d) % 2
                    settle(sp, turn)
                    sp.dma_start(out_steps[count(turn, s - d, 1)], y_norm[:, k]).then_inc(stored[k], 16)

            run(sp, part)
            for k in range(2):
                sp.wait_ge(stored[k], 16 * STEPS // 2)

        @block.gpsimd
        def _(pool):
            for k, (t, diagonal) in enumerate(((ident, 1.0), (minus_ident, -1.0))):
                nc.gpsimd.memset(t[:], 0.0).then_inc(consts, 1)
                pool.wait_ge(consts, 2 * k + 1)
                nc.gpsimd.affine_select(out=t[:], in_=t[:], compare_op=ALU.not_equal, fill=diagonal, base=0,
                                        pattern=[[-1, P]], channel_multiplier=1).then_inc(consts, 1)

            def part(turn, s, item, n):
                if item[0] == "add":
                    g = item[1]
                    i, k = g // SUMMED, g % SUMMED
                    so_far = (SUMMED - 1) * i + k - 1
                    pool.wait_ge(probs_ready, count(turn, s, TILES, H * (g + 1)))
                    if k == 1:
                        pool.wait_ge(denoms_ready, count(turn, s, 1))
                        before = probs[:, (g - 1) % RING]
                    else:
                        pool.wait_ge(sums_added, count(turn, s, ADDS, so_far))
                        before = prob_sums[:, i]
                    nc.gpsimd.tensor_tensor(prob_sums[:, i].rearrange("p h n -> p (h n)"),
                                            before.rearrange("p h n -> p (h n)"),
                                            probs[:, g % RING].rearrange("p h n -> p (h n)"),
                                            ALU.add).then_inc(sums_added, 1)
                if item[0] == "drain":
                    pool.wait_ge(res_loaded, count(turn, s, 16))
                    pool.wait_ge(weights_loaded, 48)
                    pool.wait_ge(moments_ready, count(turn, s - 1, NB))
                    nc.gpsimd.tensor_tensor(res_bias[:], x_res[:],
                                            bo_sb[:].unsqueeze(1).broadcast_to([P, NB, E]), ALU.add).then_inc(res_bias_ready, 1)
                if item[0] == "divide":
                    pool.wait_ge(recips_ready, count(turn, s, NB))
                    pool.wait_ge(drained, count(turn, s, 1))
                    nc.gpsimd.tensor_tensor(concat[:], heads_sum[:], recips[:], ALU.mult).then_inc(concat_ready, 1)
                if item[0] == "pow":
                    pool.wait_ge(moments_ready, count(turn, s, NB))
                    pool.wait_ge(norm_ready, count(turn, s - 1, NB))
                    settle(pool, turn)
                    nc.gpsimd.tensor_scalar(var_eps[:], moments[:, :, 1], EPS, None, ALU.add).then_inc(var_ready, 1)
                    pool.wait_ge(var_ready, count(turn, s, 1))
                    pool.wait_ge(fills, 5)
                    nc.gpsimd.tensor_tensor(rstd[:], var_eps[:], minus_half[:], ALU.pow).then_inc(rstd_ready, 1)

            run(pool, part)

        @block.tensor
        def _(pe):
            pe.wait_ge(qk_weights_loaded, 32)

            def part(turn, s, item, n):
                kind = item[0]
                if kind == "scores":
                    mt, h = item[1] // H, item[1] % H
                    par, half = (s // 2) % 2, s % 2
                    t = item[1]
                    if t == 0:
                        pe.wait_ge(shift_loaded, count(turn, s, 16 * NB, 16 * NB))
                        pe.wait_ge(mask_cols_made, count(turn, s, PAIRS, PAIRS))
                    pe.wait_ge(probs_ready, count(turn, s, TILES, t - 2 if t > 2 else t - 1))
                    bank = scores[t % 3]
                    nc.tensor.matmul(bank[:], k_stack[par][:, h, mt * P:mt * P + P], q_stack[par][:, half, h, :],
                                     start=True, stop=False, skip_group_check=True)
                    nc.tensor.matmul(bank[:], minus_ident[:], mask_cols[:, s % 2, mt, :],
                                     start=False, stop=True, skip_group_check=True).then_inc(scores_ready, 1)
                if kind == "values":
                    at, g = item[1], item[2]
                    d = at - s
                    pe.wait_ge(probs_ready, count(turn, s, TILES, d * TILES + H * (g + 1)))
                    if g == 0:
                        pe.wait_ge(drained, count(turn, s, 1))
                        pe.wait_ge(v_ready, graphs(turn, s - s % 2, 1, 1))
                    for h in range(H):
                        last = nc.tensor.matmul(heads_acc[DK * h:DK * h + DK, :],
                                                values[(at // 2) % 2][:, g, DK * h:DK * h + DK], probs[:, g % RING, h, :],
                                                start=(g == 0), stop=(g == MT - 1))
                    last.then_inc(values_done, 1)
                if kind not in JOBS:
                    return
                slot = n % 2
                pe.wait_ge(job_free[slot], uses(turn, n))
                if kind == "max":
                    c, h = item[2:]
                    nxt = s + item[1]
                    if (c, h) == (0, 0) and nxt % 2 == 0:
                        pe.wait_ge(stacks_loaded, graphs(turn, nxt, 16 * STACK_DMAS, 16 * STACK_DMAS))
                    q_t, k_t = q_stack[(nxt // 2) % 2], k_stack[(nxt // 2) % 2]
                    for i in range(2):
                        last = nc.tensor.matmul(job[slot][:, i * HALF:i * HALF + HALF],
                                                q_t[0:SHIFT_ROW, nxt % 2, h, c * P:c * P + P],
                                                k_t[0:SHIFT_ROW, h, i * HALF:i * HALF + HALF], start=True, stop=True)
                elif kind == "shift":
                    pe.wait_ge(job_free[1 - slot], uses(turn, n + 1))
                    for h in range(H):
                        last = nc.tensor.transpose(job[slot][0:NB, h * P:h * P + P], row_max[:, h, :], ident[:])
                elif kind in "qk":
                    if kind == "q":
                        pe.wait_ge(x_loaded, graphs(turn, s + 2 if s >= 0 else 0, 16, 16))
                    for i in range(2):
                        last = nc.tensor.matmul(job[slot][:, i * HALF:i * HALF + HALF], (wq_sb if kind == "q" else wk_sb)[:],
                                                x_t[:, i * HALF:i * HALF + HALF], start=True, stop=True)
                elif kind == "v":
                    if s == -1:
                        pe.wait_ge(weights_loaded, 48)
                        pe.wait_ge(fills, 5)
                        pe.wait_ge(consts, 4)
                    for t in range(MT):
                        last = nc.tensor.matmul(job[slot][:, t * P:t * P + P], x_t[:, t * P:t * P + P], wv_sb[:],
                                                start=True, stop=True)
                elif kind == "denoms":
                    pe.wait_ge(sums_added, count(turn, s, ADDS))
                    for h in range(H):
                        for i in range(MT // SUMMED):
                            last = nc.tensor.matmul(job[slot][DK * h:DK * h + DK, 0:HALF], ones[:], prob_sums[:, i, h, :],
                                                    start=(i == 0), stop=(i == MT // SUMMED - 1))
                elif kind == "project":
                    pe.wait_ge(concat_ready, count(turn, s, 1))
                    for c in range(NB):
                        last = nc.tensor.matmul(job[slot][:, c * E:c * E + E], concat[:, c * P:c * P + P], wo_sb[:],
                                                start=True, stop=True)
                last.then_inc(job_full[slot], 1)

            run(pe, part)

        @block.scalar
        def _(act):
            def adds_before(turn, s, groups):
                more, g = divmod(groups, MT)
                i, k = divmod(g, SUMMED)
                return count(turn, s + more, ADDS, (SUMMED - 1) * i + (0 if k == 0 else max(k - 1, 1)))

            def part(turn, s, item, n):
                kind, slot = item[0], n % 2
                if kind == "scores":
                    t = item[1]
                    act.wait_ge(scores_ready, count(turn, s, TILES, t + 1))
                    if t % H == 0:
                        act.wait_ge(values_done, count(turn, s, MT, t // H - RING + 1))
                        act.wait_ge(sums_added, adds_before(turn, s, t // H - RING + 1))
                    nc.scalar.activation(probs[:, (t // H) % RING, t % H, :], scores[t % 3][:], ACT.Exp,
                                         scale=SCALE).then_inc(probs_ready, 1)
                if item[0] == "drain":
                    act.wait_ge(values_done, count(turn, s, MT))
                    act.wait_ge(concat_ready, count(turn, s, 1, -1))
                    nc.scalar.copy(heads_sum[:], heads_acc[:]).then_inc(drained, 1)
                if kind == "copy":
                    what = item[1]
                    act.wait_ge(job_full[slot], uses(turn, n + 2))
                    to = s + 2 if s >= 0 else 0
                    if what == "shift":
                        act.wait_ge(shift_loaded, count(turn, s + 1, 16 * NB))
                        nc.scalar.mul(shift_t[:], job[slot][0:NB, 0:H * P], -1.0).then_inc(shift_t_ready, 1)
                        act.wait_ge(shift_t_ready, count(turn, s + 1, 1, 1))
                        act.sem_inc(job_free[slot], 1)
                    elif what == "denoms":
                        act.wait_ge(recips_ready, count(turn, s - 1, NB))
                        nc.scalar.copy(denoms[:], job[slot][:, 0:HALF]).then_inc(denoms_ready, 1)
                        act.wait_ge(denoms_ready, count(turn, s, 1))
                        act.sem_inc(job_free[slot], 1)
                    elif what == "v":
                        if s >= 2:
                            act.wait_ge(values_done, count(turn, s, MT))
                        nc.scalar.copy(values[(to // 2) % 2][:].rearrange("p t e -> p (t e)"),
                                       job[slot][:]).then_inc(v_ready, 1)
                        act.wait_ge(v_ready, graphs(turn, to, 1, 1))
                        act.sem_inc(job_free[slot], 1)
                    else:
                        act.wait_ge(stacks_loaded, graphs(turn, to, 16 * STACK_DMAS))
                        nc.scalar.copy((q_hi if what == "q" else k_hi)[:], job[slot][:]).then_inc(hi_ready, 1)
                if kind == "mask_cols":
                    to, i = s + item[1], item[2]
                    act.wait_ge(adj_cols_loaded[i % 2], count(turn, to, 32, 16 * (i // 2 + 1)))
                    act.wait_ge(fills, 5)
                    nc.scalar.activation(mask_cols[:, to % 2, 2 * i:2 * i + 2, :], adj_cols_in[:, i % 2], ACT.Relu,
                                         scale=MASKED, bias=minus_masked[:]).then_inc(mask_cols_made, 1)
                if item == ("low", "k") and s == -1:
                    fill_stack(act, turn, s, "k")

            run(act, part)

        @block.vector
        def _(dve):
            nc.vector.memset(ones[:], 1.0).then_inc(fills, 1)
            nc.vector.memset(minus_half[:], -0.5).then_inc(fills, 1)
            nc.vector.memset(minus_masked[:], -MASKED).then_inc(fills, 1)
            for i in range(2):
                nc.vector.memset(k_stack[i][SHIFT_ROW:SHIFT_ROW + 1].bitcast(F32), 1.0).then_inc(fills, 1)

            def part(turn, s, item, n):
                kind, slot = item[0], n % 2
                if kind in ("max", "project"):
                    dve.wait_ge(job_full[slot], uses(turn, n + 2))
                if kind == "max":
                    to, (c, h) = s + item[1], item[2:]
                    dve.wait_ge(masks_made, count(turn, to, NB, c + 1))
                    settle(dve, turn)
                    nc.vector.tensor_tensor_reduce(out=masked_scores[:, slot, :], in0=job[slot][:],
                                                   in1=mask[:, c, :], scale=1.0, scalar=LOWEST,
                                                   op0=ALU.add, op1=ALU.max,
                                                   accum_out=row_max[:, h, c:c + 1]).then_inc(job_free[slot], 1)
                if kind == "low":
                    g_hi = graphs(turn, s + 2 if s >= 0 else 0, 2, 1 if item[1] == "q" else 2)
                    dve.wait_ge(hi_ready, g_hi)
                    hi, lo = (q_hi, q_lo) if item[1] == "q" else (k_hi, k_lo)
                    nc.vector.tensor_tensor(lo[:], job[slot][:], hi[:].bitcast(F32), ALU.subtract).then_inc(lo_ready, 1)
                    dve.wait_ge(lo_ready, g_hi)
                    dve.sem_inc(job_free[slot], 1)
                if kind == "recip":
                    c = item[1]
                    dve.wait_ge(denoms_ready, count(turn, s, 1))
                    if c == 0:
                        dve.wait_ge(concat_ready, count(turn, s, 1, -1))
                    nc.vector.reciprocal(recips[:, c * P:c * P + P], denoms[:, c * P:c * P + P]).then_inc(recips_ready, 1)
                if kind == "project":
                    dve.wait_ge(res_bias_ready, count(turn, s, 1))
                    nc.vector.tensor_tensor(y[:], job[slot][:, 0:NB * E].rearrange("p (c e) -> p c e", c=NB),
                                            res_bias[:], ALU.add).then_inc(job_free[slot], 1)
                    dve.wait_ge(job_free[slot], uses(turn, n + 2))
                    for c in range(NB):
                        nc.vector.bn_stats(stats[:, c, :], y[:, c, :]).then_inc(stats_ready, 1)
                    for c in range(NB):
                        dve.wait_ge(stats_ready, count(turn, s - 1, NB, c + 1))
                        settle(dve, turn)
                        nc.vector.bn_aggr(moments[:, c, :], stats[:, c, :]).then_inc(moments_ready, 1)
                if kind == "mask":
                    to, c = s + item[1], item[2]
                    dve.wait_ge(adj_loaded[c % 2], count(turn, to, 32, 16 * (c // 2 + 1)))
                    nc.vector.tensor_scalar(mask[:, c, :], adj_in[:, c % 2, :], 0, MASKED,
                                            ALU.is_le, ALU.mult).then_inc(masks_made, 1)
                if kind == "norm":
                    d = item[1]
                    dve.wait_ge(rstd_ready, count(turn, s - d, 1, 1))
                    if s - d >= 2:
                        dve.wait_ge(stored[(s - d) % 2], stores(turn, s - d))
                    for c in range(NB):
                        nc.vector.tensor_scalar(y_norm[:, (s - d) % 2, c, :], y[:, c, :], moments[:, c, 0:1],
                                                rstd[:, c:c + 1], ALU.subtract, ALU.mult).then_inc(norm_ready, 1)

            def stores(turn, to):
                n = 16 * (to // 2)
                return n if isinstance(turn, int) else turn * 32 + n

            run(dve, part)


def kernel(x, adj, L0_gnn_Wq, L0_gnn_Wk, L0_gnn_Wv, L0_gnn_Wo, L0_gnn_bo):
    import numpy as np
    import concourse.bacc as bacc
    from concourse.bass_utils import run_bass_kernel_spmd

    def heads_last(w):
        return np.ascontiguousarray(np.transpose(np.asarray(w), (1, 0, 2)).reshape(w.shape[1], -1))

    arrays = {
        "x": np.ascontiguousarray(x),
        "x_cols": np.ascontiguousarray(np.transpose(np.asarray(x), (0, 2, 1))),
        "adj": np.ascontiguousarray(adj),
        "adj_cols": np.ascontiguousarray(np.transpose(np.asarray(adj), (0, 2, 1))),
        "wq": heads_last(L0_gnn_Wq),
        "wk": heads_last(L0_gnn_Wk),
        "wv": heads_last(L0_gnn_Wv),
        "wo_t": np.ascontiguousarray(np.asarray(L0_gnn_Wo).T),
        "bo": np.ascontiguousarray(L0_gnn_bo),
    }
    nc = bacc.Bacc("TRN2", target_bir_lowering=False, num_devices=1)
    args = [nc.dram_tensor(name, a.shape, mybir.dt.from_np(a.dtype), kind="ExternalInput").ap()
            for name, a in arrays.items()]
    out = nc.dram_tensor("out", x.shape, F32, kind="ExternalOutput").ap()
    build_kernel(nc, *args, out)
    r = run_bass_kernel_spmd(nc, [arrays], core_ids=[0])
    return r.results[0]["out"]
```

```python
from contextlib import ExitStack

import concourse.bass as bass
from concourse import mybir

F32 = mybir.dt.float32
F32R = mybir.dt.float32r
BF16 = mybir.dt.bfloat16
I32 = mybir.dt.int32
ALU = mybir.AluOpType
ACT = mybir.ActivationFunctionType

P = 128
MASKED = -1e28
LOWEST = -1e20
EPS = 1e-5


def build_kernel(nc, x, x_cols, adj, adj_cols, wq, wk, wv, wo_t, bo, out):
    B, N, E = x.shape
    H = wq.shape[1] // 32
    DK = E // H
    SCALE = float(DK) ** -0.5
    HALF = 512
    STEPS = B * N // HALF
    NB = HALF // P
    MT = N // P
    TILES = MT * H
    LAST = STEPS - 1
    SUMMED = 4
    RING = 4
    SHIFT_ROW = 3 * DK
    STACK_DMAS = 3 * 2
    ADDS = (SUMMED - 1) * (MT // SUMMED)
    PAIRS = MT // 2
    assert (E, H, DK, N) == (128, 4, 32, 1024)

    adj_blocks = adj.rearrange("b (t p) m -> (b t) p m", p=P)
    adj_pairs = adj_cols.rearrange("b (i k p) (t q) -> b t i p k q", p=P, k=2, t=2)
    x_steps = x.rearrange("b (t c p) e -> (b t) p c e", p=P, c=NB)
    out_steps = out.rearrange("b (t c p) e -> (b t) p c e", p=P, c=NB)

    TABLE = [
        (1, ("mask", 1, 2)), (1, ("max", 1, 1, 0)), (2, ("max", 1, 1, 1)), (2, ("mask_cols", 1, 0)),
        (3, ("drain",)), (3, ("max", 1, 1, 2)), (4, ("max", 1, 1, 3)), (5, ("combine",)), (6, ("q",)),
        (6, ("copy", "q")), (9, ("low", "q")), (9, ("max", 1, 2, 0)), (10, ("mask", 1, 3)), (10, ("k",)),
        (10, ("copy", "k")), (10, ("denoms",)), (11, ("norm", 2)), (11, ("add", 1)), (11, ("copy", "denoms")),
        (12, ("low", "k")), (13, ("recip", 0)), (13, ("max", 1, 2, 1)), (14, ("max", 1, 2, 2)),
        (15, ("mask_cols", 1, 1)), (15, ("v",)), (15, ("copy", "v")), (16, ("recip", 1)), (17, ("recip", 2)),
        (17, ("max", 1, 2, 3)), (17, ("mask_cols", 1, 2)), (18, ("max", 1, 3, 0)), (18, ("add", 2)),
        (19, ("max", 1, 3, 1)), (20, ("recip", 3)), (21, ("max", 1, 3, 2)), (22, ("max", 1, 3, 3)),
        (23, ("add", 3)), (23, ("divide",)), (23, ("mask", 2, 0)), (25, ("mask", 2, 1)), (26, ("shift",)),
        (26, ("project",)), (26, ("copy", "shift")), (27, ("mask_cols", 1, 3)), (27, ("add", 5)),
        (27, ("max", 2, 0, 0)), (28, ("max", 2, 0, 1)), (30, ("max", 2, 0, 2)), (30, ("add", 6)),
        (31, ("max", 2, 0, 3)), (31, ("add", 7)), (31, ("pow",)),
    ]

    def order(s):
        after = {j: [] for j in range(TILES)}
        combine_at = next(j for j, item in TABLE if item == ("combine",))
        for j, item in TABLE:
            kind, arg = item[0], item[1] if len(item) > 1 else None
            if kind in ("q", "k", "v") or arg in ("q", "k", "v"):
                wanted = s % 2 == 0 and s < STEPS - 2
            elif kind in ("max", "mask"):
                wanted = s + arg < STEPS
            elif kind in ("mask_cols", "shift") or arg == "shift":
                wanted = s + 1 < STEPS
            elif kind == "norm":
                wanted = s >= 2
            else:
                wanted = s >= 1 or kind == "add"
            if kind == "add" and s == LAST:
                j, wanted = max(H * arg + H - 1, combine_at + 1), arg < MT - 1
            if s == LAST and (kind in ("denoms", "recip", "divide", "project") or arg == "denoms"):
                j = min(j + 5, TILES - 1)
            if wanted:
                after[j].append(item)
        items = []
        for j in range(TILES):
            items.append(("scores", j))
            if j % H == H - 1:
                g = j // H - 1
                if g >= 0:
                    items.append(("values", s, g))
                elif s >= 1:
                    items.append(("values", s - 1, MT - 1))
            items += after[j]
        return items

    JOBS = ("max", "shift", "q", "k", "v", "denoms", "project")
    BEFORE = ([("adj",), ("weights",), ("adj_cols",), ("q",), ("mask", 1, 0), ("copy", "q"), ("k",), ("mask", 1, 1),
               ("copy", "k"), ("low", "q"), ("low", "k"), ("mask", 1, 2), ("mask", 1, 3)]
              + [("mask_cols", 1, i) for i in range(PAIRS)]
              + [("max", 1, c, h) for h in range(H) for c in range(NB)]
              + [("mask", 2, 0), ("shift",), ("copy", "shift"), ("max", 2, 0, 0), ("max", 2, 0, 1), ("v",), ("copy", "v")]
              + [("max", 2, 0, 2), ("max", 2, 0, 3), ("mask", 2, 1)])
    AFTER = ([("denoms",), ("copy", "denoms"), ("values", LAST, MT - 1), ("drain",), ("norm", 2)]
             + [i for c in range(NB) for i in (("recip", c), ("divide", c))] + [("project",), ("pow",), ("norm", 1)])

    def jobs_in(items):
        return sum(i[0] in JOBS for i in items)

    first_job = {-1: 0, 0: jobs_in(BEFORE)}
    for s in range(STEPS):
        first_job[s + 1] = first_job[s] + jobs_in(order(s))
    LOOP = 3
    PER = first_job[6] - first_job[2]
    assert PER == first_job[10] - first_job[6] == first_job[14] - first_job[10] and PER % 2 == 0

    with ExitStack() as ctx:
        def sb(name, shape, dt):
            return ctx.enter_context(nc.sbuf_tensor(name, shape, dt))

        def sem(name):
            return ctx.enter_context(nc.semaphore(name))

        ident = sb("ident", [P, P], F32)
        minus_ident = sb("minus_ident", [P, P], BF16)
        ones = sb("ones", [P, DK], F32)
        wq_sb = sb("wq_sb", [P, P], F32)
        wk_sb = sb("wk_sb", [P, P], F32)
        wv_sb = sb("wv_sb", [P, P], F32)
        wo_sb = sb("wo_sb", [P, P], F32)
        bo_sb = sb("bo_sb", [P, E], F32)
        minus_half = sb("minus_half", [P, NB], F32)
        adj_in = sb("adj_in", [P, 2, N], I32)
        mask = sb("mask", [P, NB, N], BF16)
        adj_cols_in = sb("adj_cols_in", [P, 2, 2, HALF], I32)
        mask_cols = sb("mask_cols", [P, 2, MT, HALF], BF16)
        minus_masked = sb("minus_masked", [P, 1], F32)
        x_t = sb("x_t", [P, N], F32)
        q_hi = sb("q_hi", [P, N], F32R)
        q_lo = sb("q_lo", [P, N], F32R)
        k_hi = sb("k_hi", [P, N], F32R)
        k_lo = sb("k_lo", [P, N], F32R)
        q_stack = [sb(f"q_stack{i}", [SHIFT_ROW + 1, 2, H, HALF], F32R) for i in range(2)]
        k_stack = [sb(f"k_stack{i}", [SHIFT_ROW + 1, H, N], F32R) for i in range(2)]
        values = [sb(f"values{i}", [P, MT, P], F32) for i in range(2)]
        masked_scores = sb("masked_scores", [P, 2, N], BF16)
        row_max = sb("row_max", [P, H, NB], F32)
        shift_t = sb("shift_t", [NB, H * P], F32R)
        probs = sb("probs", [P, RING, H, HALF], F32)
        prob_sums = sb("prob_sums", [P, MT // SUMMED, H, HALF], F32)
        heads_sum = sb("heads_sum", [P, HALF], F32)
        denoms = sb("denoms", [P, HALF], F32)
        recips = sb("recips", [P, HALF], F32)
        concat = sb("concat", [P, HALF], F32)
        x_res = sb("x_res", [P, NB, E], F32)
        res_bias = sb("res_bias", [P, NB, E], F32)
        y = sb("y", [P, NB, E], F32)
        stats = sb("stats", [P, NB, 6], F32)
        moments = sb("moments", [P, NB, 2], F32)
        var_eps = sb("var_eps", [P, NB], F32)
        rstd = sb("rstd", [P, NB], F32)
        y_norm = sb("y_norm", [P, 2, NB, E], F32)

        job = [ctx.enter_context(nc.psum_tensor(f"job{i}", [P, N], F32)) for i in range(2)]
        scores = [ctx.enter_context(nc.psum_tensor(f"scores{i}", [P, HALF], F32)) for i in range(3)]
        heads_acc = ctx.enter_context(nc.psum_tensor("heads_acc", [P, HALF], F32))

        qk_weights_loaded = sem("qk_weights_loaded")
        weights_loaded = sem("weights_loaded")
        x_loaded = sem("x_loaded")
        res_loaded = sem("res_loaded")
        adj_loaded = [sem(f"adj_loaded{i}") for i in range(2)]
        adj_cols_loaded = [sem(f"adj_cols_loaded{i}") for i in range(2)]
        stacks_loaded = [sem(f"stacks_loaded{h}") for h in range(H)]
        shift_loaded = sem("shift_loaded")
        stored = [sem(f"stored{i}") for i in range(2)]
        sums_added = sem("sums_added")
        combined = sem("combined")
        fills = sem("fills")
        consts = sem("consts")
        masks_made = sem("masks_made")
        mask_cols_made = sem("mask_cols_made")
        job_full = [sem(f"job_full{i}") for i in range(2)]
        job_free = [sem(f"job_free{i}") for i in range(2)]
        scores_ready = sem("scores_ready")
        probs_ready = sem("probs_ready")
        values_done = sem("values_done")
        hi_ready = sem("hi_ready")
        v_ready = sem("v_ready")
        lo_ready = sem("lo_ready")
        shift_t_ready = sem("shift_t_ready")
        drained = sem("drained")
        denoms_ready = sem("denoms_ready")
        recips_ready = sem("recips_ready")
        res_bias_ready = sem("res_bias_ready")
        concat_ready = sem("concat_ready")
        stats_ready = sem("stats_ready")
        moments_ready = sem("moments_ready")
        var_ready = sem("var_ready")
        rstd_ready = sem("rstd_ready")
        norm_ready = sem("norm_ready")

        waited = sem("waited")

        block = ctx.enter_context(nc.Block())

        def count(turn, s, per, more=0):
            n = max(per * s + more, 0)
            return n if isinstance(turn, int) else turn * (4 * per) + n

        def graphs(turn, s, per, more=0):
            n = max(per * (s // 2) + more, 0)
            return n if isinstance(turn, int) else turn * (2 * per) + n

        def settle(eng, turn):
            if not isinstance(turn, int):
                eng.sem_inc(waited, 1)

        def uses(turn, n):
            return n // 2 if isinstance(turn, int) else turn * (PER // 2) + n // 2

        def run(eng, part):
            def items(turn, s, listed):
                n, of = first_job[s], {}
                for item in listed:
                    if item[0] in JOBS:
                        of[item[0]] = n
                    part(turn, s, item, of[item[1]] if item[0] in ("copy", "low") else n)
                    n += item[0] in JOBS

            items(0, -1, BEFORE)
            for s in range(2):
                items(0, s, order(s))
            with eng.Fori(0, LOOP) as turn:
                for s in range(2, 6):
                    items(turn, s, order(s))
            for s in range(4 * LOOP + 2, STEPS):
                items(0, s, order(s))
            items(0, STEPS, AFTER)

        def fill_stack(eng, turn, s, which):
            to = s + 2 if s >= 0 else 0
            hi, lo = (q_hi, q_lo) if which == "q" else (k_hi, k_lo)
            eng.wait_ge(lo_ready, graphs(turn, to, 2, 1 if which == "q" else 2))
            settle(eng, turn)
            if s >= 1:
                eng.wait_ge(scores_ready, count(turn, s, TILES))
                settle(eng, turn)
            for h in range(H):
                for row, part in enumerate((hi, lo, hi) if which == "q" else (hi, hi, lo)):
                    src = part[DK * h:DK * h + DK, :].bitcast(F32)
                    if which == "q":
                        dst = q_stack[(to // 2) % 2][DK * row:DK * row + DK, :, h, :].bitcast(F32)
                        src = src.rearrange("p (t n) -> p t n", t=2)
                    else:
                        dst = k_stack[(to // 2) % 2][DK * row:DK * row + DK, h, :].bitcast(F32)
                    eng.dma_start(dst, src).then_inc(stacks_loaded[h], 16)

        def add_group(eng, ops, turn, s, g):
            i, k = g // SUMMED, g % SUMMED
            eng.wait_ge(probs_ready, count(turn, s, TILES, H * (g + 1)))
            if k > 1:
                eng.wait_ge(sums_added, count(turn, s, ADDS, (SUMMED - 1) * i + k - 1))
                before = prob_sums[:, i]
            else:
                if i == 0:
                    eng.wait_ge(combined, count(turn, s, 1))
                else:
                    eng.wait_ge(denoms_ready, count(turn, s, 1))
                before = probs[:, (g - 1) % RING]
            ops.tensor_tensor(prob_sums[:, i].rearrange("p h n -> p (h n)"), before.rearrange("p h n -> p (h n)"),
                              probs[:, g % RING].rearrange("p h n -> p (h n)"), ALU.add).then_inc(sums_added, 1)

        @block.sync
        def _(sp):
            sp.dma_start(x_t[:], x_cols[0]).then_inc(x_loaded, 16)
            sp.dma_start(wq_sb[:], wq).then_inc(qk_weights_loaded, 16)
            sp.dma_start(wk_sb[:], wk).then_inc(qk_weights_loaded, 16)

            def part(turn, s, item, n):
                if item == ("scores", 0) and s % 2 == 0 and s < STEPS - 2:
                    sp.wait_ge(v_ready, graphs(turn, s + 2, 1))
                    settle(sp, turn)
                    sp.dma_start(x_t[:], x_cols[graphs(turn, s + 2, 1)]).then_inc(x_loaded, 16)
                if item[0] == "low" and (item[1] == "q" or s >= 0):
                    fill_stack(sp, turn, s, item[1])
                if item[0] == "weights":
                    sp.dma_start(wv_sb[:], wv).then_inc(weights_loaded, 16)
                    sp.dma_start(wo_sb[:], wo_t).then_inc(weights_loaded, 16)
                    sp.dma_start(bo_sb[:], bo.partition_broadcast(P)).then_inc(weights_loaded, 16)
                if item[0] == "adj":
                    for c in range(2):
                        sp.dma_start(adj_in[:, c, :], adj_blocks[c]).then_inc(adj_loaded[c], 16)
                if item[0] == "mask":
                    to, c = s + item[1], item[2]
                    if to + (c + 2) // NB < STEPS:
                        sp.wait_ge(masks_made, count(turn, to, NB, c + 1))
                        settle(sp, turn)
                        sp.dma_start(adj_in[:, c % 2, :],
                                     adj_blocks[count(turn, to, NB, c + 2)]).then_inc(adj_loaded[c % 2], 16)
                if item[0] == "adj_cols":
                    for i in range(2):
                        sp.dma_start(adj_cols_in[:, i], adj_pairs[0, 0, i]).then_inc(adj_cols_loaded[i], 16)
                if item[0] == "mask_cols":
                    made, i = s + item[1], (item[2] + 2) % PAIRS
                    to = made + (item[2] + 2) // PAIRS
                    if to < STEPS:
                        sp.wait_ge(mask_cols_made, count(turn, made, PAIRS, item[2] + 1))
                        settle(sp, turn)
                        sp.dma_start(adj_cols_in[:, i % 2], adj_pairs[graphs(turn, to - to % 2, 1), to % 2, i]
                                     ).then_inc(adj_cols_loaded[i % 2], 16)
                if item == ("copy", "shift"):
                    sp.wait_ge(shift_t_ready, count(turn, s + 1, 1, 1))
                    settle(sp, turn)
                    for c in range(NB):
                        dst = q_stack[((s + 1) // 2) % 2][SHIFT_ROW:SHIFT_ROW + 1, (s + 1) % 2, :, c * P:c * P + P]
                        sp.dma_start(dst.bitcast(F32), shift_t[c:c + 1, :].bitcast(F32)
                                     .rearrange("p (h n) -> p h n", h=H)).then_inc(shift_loaded, 16)
                if item == ("scores", 2):
                    sp.wait_ge(res_bias_ready, count(turn, s, 1))
                    settle(sp, turn)
                    sp.dma_start(x_res[:], x_steps[count(turn, s, 1)]).then_inc(res_loaded, 16)
                if item[0] == "norm":
                    d = item[1]
                    sp.wait_ge(norm_ready, count(turn, s - d, NB, NB))
                    k = (s - d) % 2
                    settle(sp, turn)
                    sp.dma_start(out_steps[count(turn, s - d, 1)], y_norm[:, k]).then_inc(stored[k], 16)

            run(sp, part)
            for k in range(2):
                sp.wait_ge(stored[k], 16 * STEPS // 2)

        @block.gpsimd
        def _(pool):
            for k, (t, diagonal) in enumerate(((ident, 1.0), (minus_ident, -1.0))):
                nc.gpsimd.memset(t[:], 0.0).then_inc(consts, 1)
                pool.wait_ge(consts, 2 * k + 1)
                nc.gpsimd.affine_select(out=t[:], in_=t[:], compare_op=ALU.not_equal, fill=diagonal, base=0,
                                        pattern=[[-1, P]], channel_multiplier=1).then_inc(consts, 1)
            for i in range(2):
                pool.wait_ge(consts, 4 + i)
                nc.gpsimd.memset(k_stack[i][SHIFT_ROW:SHIFT_ROW + 1].bitcast(F32), 1.0).then_inc(consts, 1)

            def part(turn, s, item, n):
                if item[0] == "add" and s < LAST:
                    add_group(pool, nc.gpsimd, turn, s, item[1])
                if item[0] == "drain":
                    pool.wait_ge(res_loaded, count(turn, s, 16))
                    pool.wait_ge(weights_loaded, 48)
                    pool.wait_ge(moments_ready, count(turn, s - 1, NB))
                    nc.gpsimd.tensor_tensor(res_bias[:], x_res[:],
                                            bo_sb[:].unsqueeze(1).broadcast_to([P, NB, E]), ALU.add).then_inc(res_bias_ready, 1)
                if item == ("divide",):
                    pool.wait_ge(recips_ready, count(turn, s, NB))
                    pool.wait_ge(drained, count(turn, s, 1))
                    nc.gpsimd.tensor_tensor(concat[:], heads_sum[:], recips[:], ALU.mult).then_inc(concat_ready, 1)
                if item[0] == "pow":
                    pool.wait_ge(moments_ready, count(turn, s, NB))
                    pool.wait_ge(norm_ready, count(turn, s - 1, NB))
                    settle(pool, turn)
                    nc.gpsimd.tensor_scalar(var_eps[:], moments[:, :, 1], EPS, None, ALU.add).then_inc(var_ready, 1)
                    pool.wait_ge(var_ready, count(turn, s, 1))
                    pool.wait_ge(fills, 3)
                    nc.gpsimd.tensor_tensor(rstd[:], var_eps[:], minus_half[:], ALU.pow).then_inc(rstd_ready, 1)

            run(pool, part)

        @block.tensor
        def _(pe):
            pe.wait_ge(qk_weights_loaded, 32)

            def part(turn, s, item, n):
                kind = item[0]
                if kind == "scores":
                    mt, h = item[1] // H, item[1] % H
                    par, half = (s // 2) % 2, s % 2
                    t = item[1]
                    if t == 0:
                        pe.wait_ge(shift_loaded, count(turn, s, 16 * NB, 16 * NB))
                        pe.wait_ge(mask_cols_made, count(turn, s, PAIRS, PAIRS))
                    pe.wait_ge(probs_ready, count(turn, s, TILES, t - 2 if t > 2 else t - 1))
                    bank = scores[t % 3]
                    nc.tensor.matmul(bank[:], minus_ident[:], mask_cols[:, s % 2, mt, :], start=True, stop=False)
                    nc.tensor.matmul(bank[:], k_stack[par][:, h, mt * P:mt * P + P], q_stack[par][:, half, h, :],
                                     start=False, stop=True).then_inc(scores_ready, 1)
                if kind == "values":
                    at, g = item[1], item[2]
                    d = at - s
                    pe.wait_ge(probs_ready, count(turn, s, TILES, d * TILES + H * (g + 1)))
                    if g == 0:
                        pe.wait_ge(drained, count(turn, s, 1))
                        pe.wait_ge(v_ready, graphs(turn, s - s % 2, 1, 1))
                    for h in range(H):
                        last = nc.tensor.matmul(heads_acc[DK * h:DK * h + DK, :],
                                                values[(at // 2) % 2][:, g, DK * h:DK * h + DK], probs[:, g % RING, h, :],
                                                start=(g == 0), stop=(g == MT - 1))
                    last.then_inc(values_done, 1)
                if kind not in JOBS:
                    return
                slot = n % 2
                pe.wait_ge(job_free[slot], uses(turn, n))
                if kind == "max":
                    c, h = item[2:]
                    nxt = s + item[1]
                    if c == 0 and nxt % 2 == 0:
                        pe.wait_ge(stacks_loaded[h], graphs(turn, nxt, 16 * STACK_DMAS, 16 * STACK_DMAS))
                    q_t, k_t = q_stack[(nxt // 2) % 2], k_stack[(nxt // 2) % 2]
                    for i in range(2):
                        last = nc.tensor.matmul(job[slot][:, i * HALF:i * HALF + HALF],
                                                q_t[0:SHIFT_ROW, nxt % 2, h, c * P:c * P + P],
                                                k_t[0:SHIFT_ROW, h, i * HALF:i * HALF + HALF], start=True, stop=True)
                elif kind == "shift":
                    if s == -1:
                        pe.wait_ge(fills, 3)
                        pe.wait_ge(consts, 6)
                    pe.wait_ge(job_free[1 - slot], uses(turn, n + 1))
                    for h in range(H):
                        last = nc.tensor.transpose(job[slot][0:NB, h * P:h * P + P], row_max[:, h, :], ident[:])
                elif kind in "qk":
                    if kind == "q":
                        pe.wait_ge(x_loaded, graphs(turn, s + 2 if s >= 0 else 0, 16, 16))
                    for i in range(2):
                        last = nc.tensor.matmul(job[slot][:, i * HALF:i * HALF + HALF], (wq_sb if kind == "q" else wk_sb)[:],
                                                x_t[:, i * HALF:i * HALF + HALF], start=True, stop=True)
                elif kind == "v":
                    if s == -1:
                        pe.wait_ge(weights_loaded, 48)
                    for t in range(MT):
                        last = nc.tensor.matmul(job[slot][:, t * P:t * P + P], x_t[:, t * P:t * P + P], wv_sb[:],
                                                start=True, stop=True)
                elif kind == "denoms":
                    if s == STEPS:
                        pe.wait_ge(sums_added, count(turn, s, ADDS, -1))
                        pe.wait_ge(probs_ready, count(turn, s, TILES))
                        summands = [prob_sums[:, 0], prob_sums[:, 1], probs[:, (MT - 1) % RING]]
                    else:
                        pe.wait_ge(combined, count(turn, s, 1))
                        summands = [prob_sums[:, 1]]
                    for h in range(H):
                        for i, summand in enumerate(summands):
                            last = nc.tensor.matmul(job[slot][DK * h:DK * h + DK, 0:HALF], ones[:], summand[:, h, :],
                                                    start=(i == 0), stop=(i == len(summands) - 1))
                elif kind == "project":
                    for c in range(NB):
                        if s == STEPS:
                            pe.wait_ge(concat_ready, count(turn, s, 1, c))
                        elif c == 0:
                            pe.wait_ge(concat_ready, count(turn, s, 1))
                        last = nc.tensor.matmul(job[slot][:, c * E:c * E + E], concat[:, c * P:c * P + P], wo_sb[:],
                                                start=True, stop=True)
                last.then_inc(job_full[slot], 1)

            run(pe, part)

        @block.scalar
        def _(act):
            def adds_before(turn, s, groups):
                more, g = divmod(groups, MT)
                i, k = divmod(g, SUMMED)
                return count(turn, s + more, ADDS, (SUMMED - 1) * i + (0 if k == 0 else max(k - 1, 1)))

            def part(turn, s, item, n):
                kind, slot = item[0], n % 2
                if kind == "scores":
                    t = item[1]
                    act.wait_ge(scores_ready, count(turn, s, TILES, t + 1))
                    if t % H == 0:
                        act.wait_ge(values_done, count(turn, s, MT, t // H - RING + 1))
                        act.wait_ge(sums_added, adds_before(turn, s, t // H - RING + 1))
                    nc.scalar.activation(probs[:, (t // H) % RING, t % H, :], scores[t % 3][:], ACT.Exp,
                                         scale=SCALE).then_inc(probs_ready, 1)
                if item[0] == "drain":
                    act.wait_ge(values_done, count(turn, s, MT))
                    act.wait_ge(concat_ready, count(turn, s, 1, -1))
                    nc.scalar.copy(heads_sum[:], heads_acc[:]).then_inc(drained, 1)
                if kind == "copy":
                    what = item[1]
                    act.wait_ge(job_full[slot], uses(turn, n + 2))
                    to = s + 2 if s >= 0 else 0
                    if what == "shift":
                        act.wait_ge(shift_loaded, count(turn, s + 1, 16 * NB))
                        nc.scalar.mul(shift_t[:], job[slot][0:NB, 0:H * P], -1.0).then_inc(shift_t_ready, 1)
                        act.wait_ge(shift_t_ready, count(turn, s + 1, 1, 1))
                        act.sem_inc(job_free[slot], 1)
                    elif what == "denoms":
                        act.wait_ge(recips_ready, count(turn, s - 1, NB))
                        nc.scalar.copy(denoms[:], job[slot][:, 0:HALF]).then_inc(denoms_ready, 1)
                        act.wait_ge(denoms_ready, count(turn, s, 1))
                        act.sem_inc(job_free[slot], 1)
                    elif what == "v":
                        if s >= 2:
                            act.wait_ge(values_done, count(turn, s, MT))
                        nc.scalar.copy(values[(to // 2) % 2][:].rearrange("p t e -> p (t e)"),
                                       job[slot][:]).then_inc(v_ready, 1)
                        act.wait_ge(v_ready, graphs(turn, to, 1, 1))
                        act.sem_inc(job_free[slot], 1)
                    else:
                        for h in range(H):
                            act.wait_ge(stacks_loaded[h], graphs(turn, to, 16 * STACK_DMAS))
                        nc.scalar.copy((q_hi if what == "q" else k_hi)[:], job[slot][:]).then_inc(hi_ready, 1)
                if kind == "mask_cols":
                    to, i = s + item[1], item[2]
                    act.wait_ge(adj_cols_loaded[i % 2], count(turn, to, 32, 16 * (i // 2 + 1)))
                    act.wait_ge(fills, 3)
                    nc.scalar.activation(mask_cols[:, to % 2, 2 * i:2 * i + 2, :], adj_cols_in[:, i % 2], ACT.Relu,
                                         scale=MASKED, bias=minus_masked[:]).then_inc(mask_cols_made, 1)
                if item == ("low", "k") and s == -1:
                    fill_stack(act, turn, s, "k")

            run(act, part)

        @block.vector
        def _(dve):
            nc.vector.memset(ones[:], 1.0).then_inc(fills, 1)
            nc.vector.memset(minus_half[:], -0.5).then_inc(fills, 1)
            nc.vector.memset(minus_masked[:], -MASKED).then_inc(fills, 1)

            def part(turn, s, item, n):
                kind, slot = item[0], n % 2
                if kind in ("max", "project"):
                    dve.wait_ge(job_full[slot], uses(turn, n + 2))
                if kind == "max":
                    to, (c, h) = s + item[1], item[2:]
                    dve.wait_ge(masks_made, count(turn, to, NB, c + 1))
                    settle(dve, turn)
                    nc.vector.tensor_tensor_reduce(out=masked_scores[:, slot, :], in0=job[slot][:],
                                                   in1=mask[:, c, :], scale=1.0, scalar=LOWEST,
                                                   op0=ALU.add, op1=ALU.max,
                                                   accum_out=row_max[:, h, c:c + 1]).then_inc(job_free[slot], 1)
                if kind == "low":
                    g_hi = graphs(turn, s + 2 if s >= 0 else 0, 2, 1 if item[1] == "q" else 2)
                    dve.wait_ge(hi_ready, g_hi)
                    hi, lo = (q_hi, q_lo) if item[1] == "q" else (k_hi, k_lo)
                    nc.vector.tensor_tensor(lo[:], job[slot][:], hi[:].bitcast(F32), ALU.subtract).then_inc(lo_ready, 1)
                    dve.wait_ge(lo_ready, g_hi)
                    dve.sem_inc(job_free[slot], 1)
                if kind == "add" and s == LAST:
                    add_group(dve, nc.vector, turn, s, item[1])
                if kind == "combine":
                    dve.wait_ge(sums_added, count(turn, s, ADDS))
                    nc.vector.tensor_tensor(prob_sums[:, 1].rearrange("p h n -> p (h n)"),
                                            prob_sums[:, 0].rearrange("p h n -> p (h n)"),
                                            prob_sums[:, 1].rearrange("p h n -> p (h n)"), ALU.add).then_inc(combined, 1)
                if kind == "recip":
                    c = item[1]
                    dve.wait_ge(denoms_ready, count(turn, s, 1))
                    if c == 0:
                        dve.wait_ge(concat_ready, count(turn, s, 1, -1))
                    nc.vector.reciprocal(recips[:, c * P:c * P + P], denoms[:, c * P:c * P + P]).then_inc(recips_ready, 1)
                if kind == "divide" and s == STEPS:
                    c = item[1]
                    dve.wait_ge(recips_ready, count(turn, s - 1, NB, c + 1))
                    dve.wait_ge(drained, count(turn, s, 1))
                    nc.vector.tensor_tensor(concat[:, c * P:c * P + P], heads_sum[:, c * P:c * P + P],
                                            recips[:, c * P:c * P + P], ALU.mult).then_inc(concat_ready, 1)
                if kind == "project":
                    dve.wait_ge(res_bias_ready, count(turn, s, 1))
                    nc.vector.tensor_tensor(y[:], job[slot][:, 0:NB * E].rearrange("p (c e) -> p c e", c=NB),
                                            res_bias[:], ALU.add).then_inc(job_free[slot], 1)
                    dve.wait_ge(job_free[slot], uses(turn, n + 2))
                    for c in range(NB):
                        nc.vector.bn_stats(stats[:, c, :], y[:, c, :]).then_inc(stats_ready, 1)
                    for c in range(NB):
                        dve.wait_ge(stats_ready, count(turn, s - 1, NB, c + 1))
                        settle(dve, turn)
                        nc.vector.bn_aggr(moments[:, c, :], stats[:, c, :]).then_inc(moments_ready, 1)
                if kind == "mask":
                    to, c = s + item[1], item[2]
                    dve.wait_ge(adj_loaded[c % 2], count(turn, to, 32, 16 * (c // 2 + 1)))
                    nc.vector.tensor_scalar(mask[:, c, :], adj_in[:, c % 2, :], 0, MASKED,
                                            ALU.is_le, ALU.mult).then_inc(masks_made, 1)
                if kind == "norm":
                    d = item[1]
                    dve.wait_ge(rstd_ready, count(turn, s - d, 1, 1))
                    if s - d >= 2:
                        dve.wait_ge(stored[(s - d) % 2], stores(turn, s - d))
                    for c in range(NB):
                        nc.vector.tensor_scalar(y_norm[:, (s - d) % 2, c, :], y[:, c, :], moments[:, c, 0:1],
                                                rstd[:, c:c + 1], ALU.subtract, ALU.mult).then_inc(norm_ready, 1)

            def stores(turn, to):
                n = 16 * (to // 2)
                return n if isinstance(turn, int) else turn * 32 + n

            run(dve, part)


def kernel(x, adj, L0_gnn_Wq, L0_gnn_Wk, L0_gnn_Wv, L0_gnn_Wo, L0_gnn_bo):
    import numpy as np
    import concourse.bacc as bacc
    from concourse.bass_utils import run_bass_kernel_spmd

    def heads_last(w):
        return np.ascontiguousarray(np.transpose(np.asarray(w), (1, 0, 2)).reshape(w.shape[1], -1))

    arrays = {
        "x": np.ascontiguousarray(x),
        "x_cols": np.ascontiguousarray(np.transpose(np.asarray(x), (0, 2, 1))),
        "adj": np.ascontiguousarray(adj),
        "adj_cols": np.ascontiguousarray(np.transpose(np.asarray(adj), (0, 2, 1))),
        "wq": heads_last(L0_gnn_Wq),
        "wk": heads_last(L0_gnn_Wk),
        "wv": heads_last(L0_gnn_Wv),
        "wo_t": np.ascontiguousarray(np.asarray(L0_gnn_Wo).T),
        "bo": np.ascontiguousarray(L0_gnn_bo),
    }
    nc = bacc.Bacc("TRN2", target_bir_lowering=False, num_devices=1)
    args = [nc.dram_tensor(name, a.shape, mybir.dt.from_np(a.dtype), kind="ExternalInput").ap()
            for name, a in arrays.items()]
    out = nc.dram_tensor("out", x.shape, F32, kind="ExternalOutput").ap()
    build_kernel(nc, *args, out)
    r = run_bass_kernel_spmd(nc, [arrays], core_ids=[0])
    return r.results[0]["out"]
```
